# Optimizing a Trainium2 kernel written in Bass

```python
import numpy as np
import jax
import jax.numpy as jnp

def _softmax(x, axis=-1):
    return jax.nn.softmax(x, axis=axis)

def _gelu(x):
    return jax.nn.gelu(x, approximate=True)

def _silu(x):
    return jax.nn.silu(x)

def _sigmoid(x):
    return jax.nn.sigmoid(x)

def _layernorm(x, axis=-1, eps=1e-05):
    m = jnp.mean(x, axis=axis, keepdims=True)
    v = jnp.var(x, axis=axis, keepdims=True)
    return (x - m) / jnp.sqrt(v + eps)

def _scatter_add(tgt, idx, src, axis=0):
    return tgt.at[idx].add(src)

def _segment_sum(src, seg, n):
    return jax.ops.segment_sum(src, seg, n)
kernel_name = 'mk_cond_resid_d1_seqx_r8_4de8da'

def setup_inputs(seed: int=0):
    np.random.seed(seed)
    _w = jnp.asarray

    def _rec_inputs():
        import jax
        import jax.numpy as jnp
        _rk = jax.random.key(seed)
        x = -0.0005207 + 1.001 * jax.random.normal(jax.random.fold_in(_rk, 1), (8, 128, 128), jnp.float32)
        _lenS = 128 - jax.random.randint(jax.random.fold_in(_rk, 7), (8,), 0, max(1, 128 // 4) + 1, jnp.int32)
        _lenS2 = 128 - jax.random.randint(jax.random.fold_in(_rk, 8), (8,), 0, max(1, 128 // 4) + 1, jnp.int32)
        fside_Bx8_0 = jax.random.uniform(jax.random.fold_in(_rk, 11), (8, 8), jnp.float32, 0.0, 0.556406)
        condB_sharedgateprob = jax.random.uniform(jax.random.fold_in(_rk, 12), (8,), jnp.float32, 0.0, 0.794948)
        return (x, fside_Bx8_0, condB_sharedgateprob)
    x, fside_Bx8_0, condB_sharedgateprob = _rec_inputs()

    def _L0_cond_setup():
        import jax, jax.numpy as jnp
        import numpy as np
        E, B, S, D, F = (8, 2, 128, 128, 512)
        key = jax.random.key(seed)
        ks = jax.random.split(key, 9)
        sc_d = 1.0 / np.sqrt(D)
        sc_f = 1.0 / np.sqrt(F)
        hidden_states = jax.random.normal(ks[0], (B, S, D), dtype=jnp.float32)
        gating_probs = jax.nn.softmax(jax.random.normal(ks[1], (B, E), dtype=jnp.float32), axis=-1)
        shared_gate_prob = jax.nn.sigmoid(jax.random.normal(ks[2], (B, 1), dtype=jnp.float32))
        Wg = jax.random.normal(ks[3], (E, D, F), dtype=jnp.float32) * sc_d
        Wu = jax.random.normal(ks[4], (E, D, F), dtype=jnp.float32) * sc_d
        Wd = jax.random.normal(ks[5], (E, F, D), dtype=jnp.float32) * sc_f
        Sg = jax.random.normal(ks[6], (D, F), dtype=jnp.float32) * sc_d
        Su = jax.random.normal(ks[7], (D, F), dtype=jnp.float32) * sc_d
        Sd = jax.random.normal(ks[8], (F, D), dtype=jnp.float32) * sc_f
        return {'hidden_states': hidden_states, 'gating_probs': gating_probs, 'shared_gate_prob': shared_gate_prob, 'Wg': Wg, 'Wu': Wu, 'Wd': Wd, 'Sg': Sg, 'Su': Su, 'Sd': Sd}
    _L0_cond_all = _L0_cond_setup()
    _L0_cond_in = {k: v for k, v in _L0_cond_all.items() if k in ('Wg', 'Wu', 'Wd', 'Sg', 'Su', 'Sd')}
    del _L0_cond_all
    return {'x': x, 'fside_Bx8_0': fside_Bx8_0, 'condB_sharedgateprob': condB_sharedgateprob, 'L0_cond_Wg': _L0_cond_in['Wg'], 'L0_cond_Wu': _L0_cond_in['Wu'], 'L0_cond_Wd': _L0_cond_in['Wd'], 'L0_cond_Sg': _L0_cond_in['Sg'], 'L0_cond_Su': _L0_cond_in['Su'], 'L0_cond_Sd': _L0_cond_in['Sd']}

def reference(x, fside_Bx8_0, condB_sharedgateprob, L0_cond_Wg, L0_cond_Wu, L0_cond_Wd, L0_cond_Sg, L0_cond_Su, L0_cond_Sd):
    import jax
    import jax.numpy as jnp

    def _L0_cond_ref(hidden_states, gating_probs, shared_gate_prob, Wg, Wu, Wd, Sg, Su, Sd):
        import jax, jax.numpy as jnp
        import numpy as np
        E, B, S, D, F = (8, 2, 128, 128, 512)
        h = hidden_states
        g = jnp.einsum('bsd,edf->ebsf', h, Wg)
        u = jnp.einsum('bsd,edf->ebsf', h, Wu)
        expert_outs = jnp.einsum('ebsf,efd->ebsd', jax.nn.silu(g) * u, Wd)
        expert_output = jnp.einsum('be,ebsd->bsd', gating_probs, expert_outs)
        shared = jnp.einsum('bsf,fd->bsd', jax.nn.silu(h @ Sg) * (h @ Su), Sd)
        sg = shared_gate_prob[:, :, None]
        return (1.0 - sg) * expert_output + sg * shared
    x = x + _L0_cond_ref(x, fside_Bx8_0, condB_sharedgateprob[:, None], L0_cond_Wg, L0_cond_Wu, L0_cond_Wd, L0_cond_Sg, L0_cond_Su, L0_cond_Sd)
    return x

_drawn_inputs = setup_inputs


def setup_inputs(seed=0):
    import zlib

    import numpy as np

    out = dict(_drawn_inputs(seed))
    spreads = {}
    factors = {}
    for name, (base, spread) in spreads.items():
        noise = np.random.default_rng([zlib.crc32(name.encode()), seed]).standard_normal(out[name].shape)
        drawn = base * np.exp(spread * noise) if base else spread * noise
        out[name] = jnp.asarray(drawn.astype(out[name].dtype))
    for name, factor in factors.items():
        out[name] = (out[name] * factor).astype(out[name].dtype)
    return out
```

```python
from contextlib import ExitStack

import concourse.bass as bass
from concourse import mybir

FP32 = mybir.dt.float32
FP32R = mybir.dt.float32r
BF16 = mybir.dt.bfloat16
ALU = mybir.AluOpType
ACT = mybir.ActivationFunctionType

P = 128
HALVES = 2
LAG = 2
BANKS = 2
HB = 4
GATE, UP, DOWN = range(3)
DMA = 16
WARM_UP = 9


def build(nc, x, gates, shared_gate, Wg, Wu, Wd, Sg, Su, Sd, out):
    B, S, D = x.shape
    E, _, F = Wg.shape
    assert S == P and D == P and F % P == 0
    NF = F // P
    UNITS = NF * HALVES
    HBATCH = B // HALVES
    N = HBATCH * S
    PAIRS = E // 2
    LAST = (E + 1) * UNITS - 1
    assert E % 2 == 0 and UNITS % HB == 0 and UNITS % BANKS == 0

    ctx = ExitStack()
    with ctx:
        def sbuf(name, shape, dtype):
            return ctx.enter_context(nc.sbuf_tensor(name, shape, dtype))

        def sem(name):
            return ctx.enter_context(nc.semaphore(name))

        x_nat = sbuf("x_nat", [P, B, D], FP32)
        x_t = sbuf("x_t", [P, HALVES, N], FP32)
        x_hi = sbuf("x_hi", [P, HALVES, N], FP32R)
        x_lo = sbuf("x_lo", [P, HALVES, N], FP32R)
        xs = sbuf("xs", [P, HALVES, N], FP32)
        xs_hi = [sbuf(f"xs_hi{i}", [P, HALVES, N], FP32R) for i in range(2)]
        xs_lo = [sbuf(f"xs_lo{i}", [P, HALVES, N], FP32R) for i in range(2)]
        w_raw = [sbuf(f"w_raw{i}", [P, NF, 3, P], FP32) for i in range(2)]
        w_hi = [sbuf(f"w_hi{i}", [P, NF, 3, P], FP32R) for i in range(2)]
        w_lo = [sbuf(f"w_lo{i}", [P, NF, 3, P], FP32R) for i in range(2)]
        silu = [sbuf(f"silu{i}", [P, N], FP32) for i in range(2)]
        h_hi = [sbuf(f"h_hi{i}", [P, N], FP32R) for i in range(HB)]
        h_lo = [sbuf(f"h_lo{i}", [P, N], FP32R) for i in range(HB)]
        gates_sb = sbuf("gates_sb", [P, B, E], FP32)
        sg_sb = sbuf("sg_sb", [P, B], FP32)
        not_sg = sbuf("not_sg", [P, B], FP32)
        coef = sbuf("coef", [P, E + 1, B], FP32)
        ident = sbuf("ident", [P, P], FP32)
        zeros = sbuf("zeros", [P, N], BF16)
        table = sbuf("table", [P, 1], FP32)
        y_t = sbuf("y_t", [P, HALVES, N], FP32)
        out_sb = sbuf("out_sb", [P, B, D], FP32)

        def banks(name, n):
            return [ctx.enter_context(nc.psum_tensor(f"{name}{i}", [P, N], FP32)) for i in range(n)]

        y_ps = banks("y_ps", HALVES)
        g_ps = banks("g_ps", BANKS)
        u_ps = banks("u_ps", BANKS)
        h_ps = banks("h_ps", BANKS)

        x_loaded = [sem(f"x_loaded{h}") for h in range(HALVES)]
        gates_loaded = sem("gates_loaded")
        first_w_loaded = [sem(f"first_w_loaded{k}") for k in range(3)]
        w_loaded = [sem(f"w_loaded{i}") for i in range(2)]
        zeros_set = sem("zeros_set")
        ident_zeroed = sem("ident_zeroed")
        ident_built = sem("ident_built")
        one_minus = sem("one_minus")
        coef_ready = sem("coef_ready")
        x_transposed = sem("x_transposed")
        x_hi_done = sem("x_hi_done")
        x_lo_done = sem("x_lo_done")
        x_t_done = sem("x_t_done")
        first_xs_done = sem("first_xs_done")
        first_xs_lo_done = sem("first_xs_lo_done")
        first_w_hi_done = sem("first_w_hi_done")
        first_gate_lo_done = sem("first_gate_lo_done")
        first_w_lo_done = sem("first_w_lo_done")
        xs_done = sem("xs_done")
        xs_hi_done = sem("xs_hi_done")
        xs_lo_done = sem("xs_lo_done")
        w_hi_done = sem("w_hi_done")
        w_lo_done = sem("w_lo_done")
        gate_done = sem("gate_done")
        up_done = sem("up_done")
        silu_done = sem("silu_done")
        hidden_done = sem("hidden_done")
        h_hi_done = sem("h_hi_done")
        h_lo_done = sem("h_lo_done")
        down_done = sem("down_done")
        y_copied = sem("y_copied")
        y_transposed = sem("y_transposed")
        out_ready = sem("out_ready")
        out_stored = sem("out_stored")

        x_view = x.rearrange("b s d -> s b d")
        out_view = out.rearrange("b s d -> s b d")

        def half(t, h):
            return t[:, h * HBATCH:(h + 1) * HBATCH, :]

        def in_slices(w):
            return w.rearrange("d (n j) -> d n j", j=P)

        def in_rows(w):
            return w.rearrange("(n p) d -> p n d", p=P)

        def f32(t):
            return t.bitcast(FP32)

        block = ctx.enter_context(nc.Block())

        @block.sync
        def _(sp):
            sp.dma_start(half(x_nat, 0), half(x_view, 0)).then_inc(x_loaded[0], DMA)
            sp.dma_start(half(x_nat, 1), half(x_view, 1)).then_inc(x_loaded[1], DMA)
            sp.dma_start(w_raw[0][:, :, DOWN, :], in_rows(Sd)).then_inc(first_w_loaded[DOWN], DMA)

            def load_expert(r, buf):
                sp.dma_start(w_raw[buf][:, :, GATE, :], in_slices(Wg[r])).then_inc(w_loaded[buf], DMA)
                sp.dma_start(w_raw[buf][:, :, UP, :], in_slices(Wu[r])).then_inc(w_loaded[buf], DMA)
                sp.dma_start(w_raw[buf][:, :, DOWN, :], in_rows(Wd[r])).then_inc(w_loaded[buf], DMA)

            load_expert(0, 1)
            sp.wait_ge(first_w_hi_done, 3)
            sp.wait_ge(first_gate_lo_done, 1)
            sp.wait_ge(first_w_lo_done, 2)
            load_expert(1, 0)
            with sp.Fori(0, PAIRS - 1) as i:
                sp.wait_ge(w_lo_done, 2 * NF * i + NF)
                load_expert(2 * i + 2, 1)
                sp.wait_ge(w_lo_done, 2 * NF * i + 2 * NF)
                load_expert(2 * i + 3, 0)

            for h in range(HALVES):
                sp.wait_ge(out_ready, h + 1)
                sp.dma_start(half(out_view, h), half(out_sb, h)).then_inc(out_stored, DMA)
            sp.wait_ge(out_stored, HALVES * DMA)

        @block.gpsimd
        def _(pool):
            pool.memset(ident[:, :], 0.0).then_inc(ident_zeroed, 1)
            pool.wait_ge(ident_zeroed, 1)
            pool.affine_select(out=ident[:, :], in_=ident[:, :], compare_op=ALU.not_equal, fill=1.0,
                               base=0, pattern=[[-1, P]], channel_multiplier=1).then_inc(ident_built, 1)
            for k in (UP, DOWN):
                pool.wait_ge(first_w_hi_done, k + 1)
                pool.tensor_tensor(w_lo[0][:, :, k, :], w_raw[0][:, :, k, :], f32(w_hi[0][:, :, k, :]),
                                   ALU.subtract).then_inc(first_w_lo_done, 1)

            def prepare(e, buf, halves_before, slices_before, second):
                for h in range(HALVES):
                    pool.wait_ge(xs_hi_done, halves_before + h + 1)
                    if second:
                        pool.wait_ge(xs_lo_done, halves_before - HALVES + h + 1)
                    else:
                        pool.wait_ge(first_xs_lo_done, h + 1)
                    c = coef[:, e, h * HBATCH:(h + 1) * HBATCH]
                    pool.tensor_tensor(
                        xs[:, h, :].rearrange("p (b s) -> p b s", b=HBATCH),
                        x_t[:, h, :].rearrange("p (b s) -> p b s", b=HBATCH),
                        c.unsqueeze(2).to_broadcast([P, HBATCH, S]), ALU.mult).then_inc(xs_done, 1)

                def slice_lo(n):
                    pool.wait_ge(w_hi_done, slices_before + n + 1)
                    pool.tensor_tensor(w_lo[buf][:, n, :, :], w_raw[buf][:, n, :, :],
                                       f32(w_hi[buf][:, n, :, :]), ALU.subtract).then_inc(w_lo_done, 1)

                slice_lo(0)
                for h in range(HALVES):
                    pool.wait_ge(xs_hi_done, halves_before + HALVES + h + 1)
                    pool.tensor_tensor(xs_lo[buf][:, h, :], xs[:, h, :], f32(xs_hi[buf][:, h, :]),
                                       ALU.subtract).then_inc(xs_lo_done, 1)
                for n in range(1, NF):
                    slice_lo(n)

            pool.wait_ge(x_t_done, HALVES)
            pool.wait_ge(coef_ready, 2)
            prepare(1, 1, 0, 0, second=False)
            with pool.Fori(0, PAIRS - 1) as i:
                for q in range(2):
                    prepare(2 * i + 2 + q, q, 2 * HALVES * i + HALVES * (q + 1),
                            2 * NF * i + NF * (q + 1), second=True)
            prepare(E, 0, HALVES * (E - 1), NF * (E - 1), second=True)

        @block.scalar
        def _(act):
            act.dma_start(w_raw[0][:, :, GATE, :], in_slices(Sg)).then_inc(first_w_loaded[GATE], DMA)
            act.dma_start(w_raw[0][:, :, UP, :], in_slices(Su)).then_inc(first_w_loaded[UP], DMA)
            act.dma_start(sg_sb[:, :], shared_gate.partition_broadcast(P)).then_inc(gates_loaded, DMA)
            act.dma_start(gates_sb[:, :, :], gates.partition_broadcast(P)).then_inc(gates_loaded, DMA)
            act.wait_ge(zeros_set, 1)
            act.activation(table[:, :], zeros[:, 0:1], ACT.Silu)

            def first_hi(k):
                act.wait_ge(first_w_loaded[k], DMA)
                act.activation(w_hi[0][:, :, k, :], w_raw[0][:, :, k, :], ACT.Copy)\
                   .then_inc(first_w_hi_done, 1)

            def first_x_hi(h):
                act.wait_ge(x_transposed, h + 1)
                act.activation(x_hi[:, h, :], h_ps[h][:, :], ACT.Copy).then_inc(x_hi_done, 1)

            def first_xs_hi(h):
                act.wait_ge(first_xs_done, h + 1)
                act.activation(xs_hi[0][:, h, :], xs[:, h, :], ACT.Copy).then_inc(xs_hi_done, 1)

            first_hi(GATE)
            first_x_hi(0)
            first_hi(UP)
            first_xs_hi(0)
            first_x_hi(1)
            first_xs_hi(1)
            first_hi(DOWN)

            def xs_hi_half(h, buf, halves_before):
                act.wait_ge(xs_done, halves_before + h + 1)
                act.activation(xs_hi[buf][:, h, :], xs[:, h, :], ACT.Copy).then_inc(xs_hi_done, 1)

            def w_hi_slice(n, buf, loads):
                act.wait_ge(w_loaded[buf], 3 * DMA * loads)
                act.activation(w_hi[buf][:, n, :, :], w_raw[buf][:, n, :, :], ACT.Copy)\
                   .then_inc(w_hi_done, 1)

            def expert(base, nxt, first=False):
                for k in range(UNITS):
                    act.wait_ge(gate_done, base + k + 1)
                    if not first or k >= 2:
                        act.wait_ge(hidden_done, base + k - 1)
                    act.activation(silu[k % 2][:, :], g_ps[k % BANKS][:, :], ACT.Silu)\
                       .then_inc(silu_done, 1)
                    if nxt is not None and k >= LAG:
                        buf, halves_before, loads = nxt
                        if k == LAG and not first:
                            act.wait_ge(down_done, base)
                        if k == LAG:
                            w_hi_slice(0, buf, loads)
                        elif k <= LAG + HALVES:
                            xs_hi_half(k - LAG - 1, buf, halves_before)
                        else:
                            w_hi_slice(k - LAG - HALVES, buf, loads)
                    act.wait_ge(hidden_done, base + k + 1)
                    if not first or k >= HB:
                        act.wait_ge(down_done, base + k - HB + 1)
                    act.activation(h_hi[k % HB][:, :], h_ps[k % BANKS][:, :], ACT.Copy)\
                       .then_inc(h_hi_done, 1)

            expert(0, (1, 0, 1), first=True)
            with act.Fori(0, PAIRS - 1) as i:
                base = 2 * UNITS * i + UNITS
                expert(base, (0, 2 * HALVES * i + HALVES, i + 1))
                expert(base + UNITS, (1, 2 * HALVES * i + 2 * HALVES, i + 2))
            expert((E - 1) * UNITS, (0, (E - 1) * HALVES, PAIRS))
            expert(E * UNITS, None)

            for h in range(HALVES):
                act.wait_ge(down_done, LAST + h)
                act.activation(y_t[:, h, :], y_ps[h][:, :], ACT.Copy).then_inc(y_copied, 1)

        @block.vector
        def _(dve):
            dve.memset(zeros[:, :], 0.0).then_inc(zeros_set, 1)

            dve.wait_ge(gates_loaded, 2 * DMA)
            dve.tensor_copy(coef[:, 0, :], sg_sb[:, :]).then_inc(coef_ready, 1)
            dve.tensor_scalar(not_sg[:, :], sg_sb[:, :], -1.0, 1.0, ALU.mult, ALU.add)\
               .then_inc(one_minus, 1)
            dve.wait_ge(one_minus, 1)
            dve.tensor_tensor(coef[:, 1:, :].rearrange("p e b -> p b e"), gates_sb[:, :, :],
                              not_sg[:, :].unsqueeze(2).to_broadcast([P, B, E]), ALU.mult)\
               .then_inc(coef_ready, 1)

            dve.wait_ge(first_w_hi_done, GATE + 1)
            dve.tensor_tensor(w_lo[0][:, :, GATE, :], w_raw[0][:, :, GATE, :],
                              f32(w_hi[0][:, :, GATE, :]), ALU.subtract).then_inc(first_gate_lo_done, 1)
            dve.wait_ge(coef_ready, 1)
            for h in range(HALVES):
                dve.wait_ge(x_transposed, h + 1)
                dve.wait_ge(x_hi_done, h + 1)
                dve.tensor_tensor(x_lo[:, h, :], h_ps[h][:, :], f32(x_hi[:, h, :]), ALU.subtract)\
                   .then_inc(x_lo_done, 1)
                c = coef[:, 0, h * HBATCH:(h + 1) * HBATCH]
                dve.tensor_tensor(xs[:, h, :].rearrange("p (b s) -> p b s", b=HBATCH),
                                  h_ps[h][:, :].rearrange("p (b s) -> p b s", b=HBATCH),
                                  c.unsqueeze(2).to_broadcast([P, HBATCH, S]), ALU.mult)\
                   .then_inc(first_xs_done, 1)
                dve.wait_ge(first_xs_done, h + 1)
                dve.wait_ge(xs_hi_done, h + 1)
                dve.tensor_tensor(xs_lo[0][:, h, :], xs[:, h, :], f32(xs_hi[0][:, h, :]), ALU.subtract)\
                   .then_inc(first_xs_lo_done, 1)
            for h in range(HALVES):
                dve.tensor_copy(x_t[:, h, :], h_ps[h][:, :]).then_inc(x_t_done, 1)

            def hidden(n, k, first=False):
                dve.wait_ge(silu_done, n + 1)
                dve.wait_ge(up_done, n + 1)
                if not first:
                    dve.wait_ge(h_lo_done, n - BANKS + 1)
                else:
                    dve.wait_ge(x_t_done, k + 1)
                dve.tensor_tensor(h_ps[k % BANKS][:, :], silu[k % 2][:, :], u_ps[k % BANKS][:, :],
                                  ALU.mult).then_inc(hidden_done, 1)

            def hidden_lo(n, k):
                dve.wait_ge(h_hi_done, n + 1)
                dve.tensor_tensor(h_lo[k % HB][:, :], h_ps[k % BANKS][:, :], f32(h_hi[k % HB][:, :]),
                                  ALU.subtract).then_inc(h_lo_done, 1)

            for k in range(UNITS):
                hidden(k, k, first=k < BANKS)
                if k >= 1:
                    hidden_lo(k - 1, k - 1)
            with dve.Fori(1, E + 1) as e:
                for k in range(UNITS):
                    hidden(UNITS * e + k, k)
                    hidden_lo(UNITS * e + k - 1, (k - 1) % UNITS)
            hidden_lo(LAST, UNITS - 1)

            for h in range(HALVES):
                dve.wait_ge(y_transposed, h + 1)
                dve.tensor_tensor(half(out_sb, h), h_ps[h][:, :].rearrange("p (b d) -> p b d", b=HBATCH),
                                  half(x_nat, h), ALU.add).then_inc(out_ready, 1)

        @block.tensor
        def _(pe):
            pe.wait_ge(zeros_set, 1)
            for _ in range(WARM_UP):
                pe.matmul(y_ps[0][:, :], zeros[:, 0:P], zeros[:, :], start=True, stop=True)

            pe.wait_ge(ident_built, 1)
            for h in range(HALVES):
                pe.wait_ge(x_loaded[h], DMA)
                for b in range(HBATCH):
                    last = pe.transpose(h_ps[h][:, b * S:(b + 1) * S], x_nat[:, h * HBATCH + b, :],
                                        ident[:, :])
                last.then_inc(x_transposed, 1)

            def down(n, k, buf, begin=False, end=False):
                f, h = divmod(k, HALVES)
                hi, lo = w_hi[buf][:, f, DOWN, :], w_lo[buf][:, f, DOWN, :]
                pe.wait_ge(h_hi_done, n + 1)
                pe.matmul(y_ps[h][:, :], hi, h_hi[k % HB][:, :], start=begin, stop=False)
                pe.matmul(y_ps[h][:, :], lo, h_hi[k % HB][:, :], start=False, stop=False)
                pe.wait_ge(h_lo_done, n + 1)
                pe.matmul(y_ps[h][:, :], hi, h_lo[k % HB][:, :], start=False, stop=end)\
                  .then_inc(down_done, 1)

            def shared_expert():
                for k in range(UNITS):
                    f, h = divmod(k, HALVES)
                    g, u = g_ps[k % BANKS], u_ps[k % BANKS]
                    if k >= BANKS:
                        pe.wait_ge(silu_done, k - BANKS + 1)
                    pe.wait_ge(first_w_hi_done, GATE + 1)
                    pe.wait_ge(x_hi_done, h + 1)
                    pe.matmul(g[:, :], w_hi[0][:, f, GATE, :], x_hi[:, h, :], start=True, stop=False)
                    pe.wait_ge(first_gate_lo_done, 1)
                    pe.matmul(g[:, :], w_lo[0][:, f, GATE, :], x_hi[:, h, :], start=False, stop=False)
                    pe.wait_ge(x_lo_done, h + 1)
                    pe.matmul(g[:, :], w_hi[0][:, f, GATE, :], x_lo[:, h, :], start=False, stop=True)\
                      .then_inc(gate_done, 1)
                    if k >= BANKS:
                        pe.wait_ge(hidden_done, k - BANKS + 1)
                    pe.wait_ge(first_w_hi_done, UP + 1)
                    pe.wait_ge(xs_hi_done, h + 1)
                    pe.matmul(u[:, :], w_hi[0][:, f, UP, :], xs_hi[0][:, h, :], start=True, stop=False)
                    pe.wait_ge(first_w_lo_done, 1)
                    pe.matmul(u[:, :], w_lo[0][:, f, UP, :], xs_hi[0][:, h, :], start=False, stop=False)
                    pe.wait_ge(first_xs_lo_done, h + 1)
                    pe.matmul(u[:, :], w_hi[0][:, f, UP, :], xs_lo[0][:, h, :], start=False, stop=True)\
                      .then_inc(up_done, 1)
                    if k == LAG:
                        pe.wait_ge(first_w_hi_done, DOWN + 1)
                        pe.wait_ge(first_w_lo_done, 2)
                    if k >= LAG:
                        down(k - LAG, k - LAG, 0, begin=k - LAG < HALVES)

            def routed_expert(base, buf, halves_before, slices_before):
                for k in range(UNITS):
                    f, h = divmod(k, HALVES)
                    g, u = g_ps[k % BANKS], u_ps[k % BANKS]
                    if h == 0:
                        pe.wait_ge(w_lo_done, slices_before + f + 1)
                    if f == 0:
                        pe.wait_ge(xs_lo_done, halves_before + h + 1)
                    pe.wait_ge(silu_done, base + k - BANKS + 1)
                    hi, lo = w_hi[buf][:, f, GATE, :], w_lo[buf][:, f, GATE, :]
                    pe.matmul(g[:, :], hi, x_hi[:, h, :], start=True, stop=False)
                    pe.matmul(g[:, :], hi, x_lo[:, h, :], start=False, stop=False)
                    pe.matmul(g[:, :], lo, x_hi[:, h, :], start=False, stop=True).then_inc(gate_done, 1)
                    pe.wait_ge(hidden_done, base + k - BANKS + 1)
                    hi, lo = w_hi[buf][:, f, UP, :], w_lo[buf][:, f, UP, :]
                    pe.matmul(u[:, :], hi, xs_hi[buf][:, h, :], start=True, stop=False)
                    pe.matmul(u[:, :], hi, xs_lo[buf][:, h, :], start=False, stop=False)
                    pe.matmul(u[:, :], lo, xs_hi[buf][:, h, :], start=False, stop=True)\
                      .then_inc(up_done, 1)
                    down(base + k - LAG, (k - LAG) % UNITS, buf if k >= LAG else 1 - buf)

            shared_expert()
            with pe.Fori(0, PAIRS) as i:
                for q in range(2):
                    routed_expert(2 * UNITS * i + UNITS * (q + 1), 1 - q,
                                  2 * HALVES * i + HALVES * q, 2 * NF * i + NF * q)
            for n in range(LAG):
                down(LAST - LAG + 1 + n, UNITS - LAG + n, 0, end=True)

            for h in range(HALVES):
                pe.wait_ge(y_copied, h + 1)
                for b in range(HBATCH):
                    last = pe.transpose(h_ps[h][:, b * S:(b + 1) * S], y_t[:, h, b * S:(b + 1) * S],
                                        ident[:, :])
                last.then_inc(y_transposed, 1)


_INS = ["x", "fside_Bx8_0", "condB_sharedgateprob", "L0_cond_Wg", "L0_cond_Wu", "L0_cond_Wd",
        "L0_cond_Sg", "L0_cond_Su", "L0_cond_Sd"]


def kernel(**inputs):
    import numpy as _np
    import concourse.bacc as _bacc
    from concourse import mybir as _mybir
    from concourse.bass_utils import run_bass_kernel_spmd as _run

    nc = _bacc.Bacc("TRN2", target_bir_lowering=False, num_devices=1)
    arrays, args = {}, []
    for name in _INS:
        a = _np.ascontiguousarray(inputs[name])
        arrays[f"in_{name}"] = a
        args.append(nc.dram_tensor(f"in_{name}", a.shape, _mybir.dt.from_np(a.dtype),
                                   kind="ExternalInput").ap())
    shape = arrays["in_x"].shape
    out = nc.dram_tensor("out", shape, _mybir.dt.float32, kind="ExternalOutput").ap()
    build(nc, *args, out)
    r = _run(nc, [arrays], core_ids=[0])
    return r.results[0]["out"]
```

```python
from contextlib import ExitStack

import concourse.bass as bass
from concourse import mybir

FP32 = mybir.dt.float32
FP32R = mybir.dt.float32r
BF16 = mybir.dt.bfloat16
ALU = mybir.AluOpType
ACT = mybir.ActivationFunctionType

P = 128
HALVES = 2
LAG = 2
BANKS = 2
HB = 4
GATE, UP, DOWN = range(3)
DMA = 16
WARM_UP = 9
WARM_UP_MORE = 1


def build(nc, x, gates, shared_gate, Wg, Wu, Wd, Sg, Su, Sd, out):
    B, S, D = x.shape
    E, _, F = Wg.shape
    assert S == P and D == P and F % P == 0
    NF = F // P
    UNITS = NF * HALVES
    HBATCH = B // HALVES
    N = HBATCH * S
    PAIRS = E // 2
    LAST = (E + 1) * UNITS - 1
    PIECES = [(0, 0, HBATCH), (1, 0, HBATCH // 2), (1, HBATCH // 2, HBATCH // 2)]
    PREPARE = [("slice", 0), ("half", 0)] + [("slice", n) for n in range(1, NF)] + [("half", 1)]
    FIRST_LO = [(UP, 0, 1), (UP, 1, NF), (DOWN, 0, NF)]
    assert E % 2 == 0 and UNITS % HB == 0 and UNITS % BANKS == 0 and LAG == BANKS and UNITS == LAG + len(PREPARE)

    ctx = ExitStack()
    with ctx:
        def sbuf(name, shape, dtype):
            return ctx.enter_context(nc.sbuf_tensor(name, shape, dtype))

        def sem(name):
            return ctx.enter_context(nc.semaphore(name))

        x_nat = sbuf("x_nat", [P, B, D], FP32)
        x_t = sbuf("x_t", [P, HALVES, N], FP32)
        x_hi = sbuf("x_hi", [P, HALVES, N], FP32R)
        x_lo = sbuf("x_lo", [P, HALVES, N], FP32R)
        xs_nat = sbuf("xs_nat", [P, HBATCH, D], FP32)
        xs = sbuf("xs", [P, HALVES, N], FP32)
        xs_hi = [sbuf(f"xs_hi{i}", [P, HALVES, N], FP32R) for i in range(2)]
        xs_lo = [sbuf(f"xs_lo{i}", [P, HALVES, N], FP32R) for i in range(2)]
        w_raw = [sbuf(f"w_raw{i}", [P, NF, 3, P], FP32) for i in range(2)]
        w_hi = [sbuf(f"w_hi{i}", [P, NF, 3, P], FP32R) for i in range(2)]
        w_lo = [sbuf(f"w_lo{i}", [P, NF, 3, P], FP32R) for i in range(2)]
        silu = [sbuf(f"silu{i}", [P, N], FP32) for i in range(2)]
        h_hi = [sbuf(f"h_hi{i}", [P, N], FP32R) for i in range(HB)]
        h_lo = [sbuf(f"h_lo{i}", [P, N], FP32R) for i in range(HB)]
        gates_sb = sbuf("gates_sb", [P, B, E], FP32)
        sg_sb = sbuf("sg_sb", [P, B], FP32)
        not_sg = sbuf("not_sg", [P, B], FP32)
        coef = sbuf("coef", [P, E + 1, B], FP32)
        ident = sbuf("ident", [P, P], FP32)
        zeros = sbuf("zeros", [P, N], BF16)
        table = sbuf("table", [P, 1], FP32)
        y_t = sbuf("y_t", [P, HALVES, N], FP32)
        out_sb = sbuf("out_sb", [P, B, D], FP32)

        def banks(name, n):
            return [ctx.enter_context(nc.psum_tensor(f"{name}{i}", [P, N], FP32)) for i in range(n)]

        y_ps = banks("y_ps", HALVES)
        g_ps = banks("g_ps", BANKS)
        u_ps = banks("u_ps", BANKS)
        h_ps = banks("h_ps", BANKS)
        back_ps = g_ps + u_ps[:1]

        x_loaded = [sem(f"x_loaded{h}") for h in range(HALVES)]
        sg_loaded = sem("sg_loaded")
        gates_loaded = sem("gates_loaded")
        first_w_loaded = [sem(f"first_w_loaded{k}") for k in range(3)]
        w_loaded = [sem(f"w_loaded{i}") for i in range(2)]
        zeros_set = sem("zeros_set")
        ident_zeroed = sem("ident_zeroed")
        ident_built = sem("ident_built")
        one_minus = sem("one_minus")
        coef_ready = sem("coef_ready")
        x_transposed = sem("x_transposed")
        xs_nat_done = sem("xs_nat_done")
        xs_transposed = sem("xs_transposed")
        x_hi_done = sem("x_hi_done")
        x_lo_done = sem("x_lo_done")
        x_t_done = sem("x_t_done")
        first_xs_done = sem("first_xs_done")
        first_xs_lo_done = sem("first_xs_lo_done")
        first_w_hi_done = sem("first_w_hi_done")
        first_gate_lo_done = sem("first_gate_lo_done")
        first_w_lo_done = sem("first_w_lo_done")
        xs_done = sem("xs_done")
        xs_hi_done = sem("xs_hi_done")
        xs_lo_done = sem("xs_lo_done")
        w_hi_done = sem("w_hi_done")
        w_lo_done = sem("w_lo_done")
        gate_done = sem("gate_done")
        up_done = sem("up_done")
        silu_done = sem("silu_done")
        hidden_done = sem("hidden_done")
        h_hi_done = sem("h_hi_done")
        h_lo_done = sem("h_lo_done")
        down_done = sem("down_done")
        y_copied = sem("y_copied")
        y_transposed = sem("y_transposed")
        out_ready = sem("out_ready")
        out_stored = sem("out_stored")

        x_view = x.rearrange("b s d -> s b d")
        out_view = out.rearrange("b s d -> s b d")

        def half(t, h):
            return t[:, h * HBATCH:(h + 1) * HBATCH, :]

        def in_slices(w):
            return w.rearrange("d (n j) -> d n j", j=P)

        def in_rows(w):
            return w.rearrange("(n p) d -> p n d", p=P)

        def f32(t):
            return t.bitcast(FP32)

        block = ctx.enter_context(nc.Block())

        @block.sync
        def _(sp):
            sp.dma_start(half(x_nat, 0), half(x_view, 0)).then_inc(x_loaded[0], DMA)
            sp.dma_start(w_raw[0][:, :, UP, :], in_slices(Su)).then_inc(first_w_loaded[UP], DMA)
            sp.dma_start(w_raw[0][:, :, DOWN, :], in_rows(Sd)).then_inc(first_w_loaded[DOWN], DMA)
            sp.dma_start(half(x_nat, 1), half(x_view, 1)).then_inc(x_loaded[1], DMA)

            def load_expert(r, buf):
                sp.dma_start(w_raw[buf][:, :, GATE, :], in_slices(Wg[r])).then_inc(w_loaded[buf], DMA)
                sp.dma_start(w_raw[buf][:, :, UP, :], in_slices(Wu[r])).then_inc(w_loaded[buf], DMA)
                sp.dma_start(w_raw[buf][:, :, DOWN, :], in_rows(Wd[r])).then_inc(w_loaded[buf], DMA)

            load_expert(0, 1)
            sp.wait_ge(first_w_hi_done, 3)
            sp.wait_ge(first_gate_lo_done, 1)
            sp.wait_ge(first_w_lo_done, len(FIRST_LO))
            load_expert(1, 0)
            with sp.Fori(0, PAIRS - 1) as i:
                sp.wait_ge(w_lo_done, 2 * NF * i + NF)
                load_expert(2 * i + 2, 1)
                sp.wait_ge(w_lo_done, 2 * NF * i + 2 * NF)
                load_expert(2 * i + 3, 0)

            for p, (h, a, n) in enumerate(PIECES):
                b = h * HBATCH + a
                sp.wait_ge(out_ready, p + 1)
                sp.dma_start(out_view[:, b:b + n, :], out_sb[:, b:b + n, :]).then_inc(out_stored, DMA)
            sp.wait_ge(out_stored, len(PIECES) * DMA)

        @block.gpsimd
        def _(pool):
            pool.dma_start(sg_sb[:, :], shared_gate.partition_broadcast(P)).then_inc(sg_loaded, DMA)
            pool.memset(ident[:, :], 0.0).then_inc(ident_zeroed, 1)
            pool.wait_ge(ident_zeroed, 1)
            pool.affine_select(out=ident[:, :], in_=ident[:, :], compare_op=ALU.not_equal, fill=1.0,
                               base=0, pattern=[[-1, P]], channel_multiplier=1).then_inc(ident_built, 1)
            pool.dma_start(gates_sb[:, :, :], gates.partition_broadcast(P)).then_inc(gates_loaded, DMA)
            for k, n, m in FIRST_LO:
                pool.wait_ge(first_w_hi_done, k + 1)
                pool.tensor_tensor(w_lo[0][:, n:m, k, :], w_raw[0][:, n:m, k, :],
                                   f32(w_hi[0][:, n:m, k, :]), ALU.subtract).then_inc(first_w_lo_done, 1)
            def tokens(h):
                pool.wait_ge(x_hi_done, h + 1)
                pool.wait_ge(x_lo_done, h + 1)
                pool.tensor_tensor(x_t[:, h, :], f32(x_hi[:, h, :]), f32(x_lo[:, h, :]), ALU.add)\
                    .then_inc(x_t_done, 1)

            def prepare(e, buf, halves_before, slices_before, second):
                for h in range(HALVES):
                    if not second:
                        tokens(h)
                        pool.wait_ge(x_t_done, h + 1)
                    pool.wait_ge(xs_hi_done, halves_before + h + 1)
                    if second:
                        pool.wait_ge(xs_lo_done, halves_before - HALVES + h + 1)
                    else:
                        pool.wait_ge(first_xs_lo_done, h + 1)
                    c = coef[:, e, h * HBATCH:(h + 1) * HBATCH]
                    pool.tensor_tensor(
                        xs[:, h, :].rearrange("p (b s) -> p b s", b=HBATCH),
                        x_t[:, h, :].rearrange("p (b s) -> p b s", b=HBATCH),
                        c.unsqueeze(2).to_broadcast([P, HBATCH, S]), ALU.mult).then_inc(xs_done, 1)

                def slice_lo(n):
                    pool.wait_ge(w_hi_done, slices_before + n + 1)
                    pool.tensor_tensor(w_lo[buf][:, n, :, :], w_raw[buf][:, n, :, :],
                                       f32(w_hi[buf][:, n, :, :]), ALU.subtract).then_inc(w_lo_done, 1)

                def half_lo(h):
                    pool.wait_ge(xs_hi_done, halves_before + HALVES + h + 1)
                    pool.tensor_tensor(xs_lo[buf][:, h, :], xs[:, h, :], f32(xs_hi[buf][:, h, :]),
                                       ALU.subtract).then_inc(xs_lo_done, 1)

                for kind, n in PREPARE:
                    (slice_lo if kind == "slice" else half_lo)(n)

            pool.wait_ge(coef_ready, 2)
            prepare(1, 1, 0, 0, second=False)
            with pool.Fori(0, PAIRS - 1) as i:
                for q in range(2):
                    prepare(2 * i + 2 + q, q, 2 * HALVES * i + HALVES * (q + 1),
                            2 * NF * i + NF * (q + 1), second=True)
            prepare(E, 0, HALVES * (E - 1), NF * (E - 1), second=True)

        @block.scalar
        def _(act):
            act.dma_start(w_raw[0][:, :, GATE, :], in_slices(Sg)).then_inc(first_w_loaded[GATE], DMA)
            act.wait_ge(zeros_set, 1)
            act.activation(table[:, :], zeros[:, 0:1], ACT.Silu)

            def first_hi(k):
                act.wait_ge(first_w_loaded[k], DMA)
                act.activation(w_hi[0][:, :, k, :], w_raw[0][:, :, k, :], ACT.Copy)\
                   .then_inc(first_w_hi_done, 1)

            def first_x_hi(h):
                act.wait_ge(x_transposed, h + 1)
                act.activation(x_hi[:, h, :], y_ps[h][:, :], ACT.Copy).then_inc(x_hi_done, 1)

            def first_xs_hi(h):
                act.wait_ge(first_xs_done if h else xs_transposed, 1)
                act.activation(xs_hi[0][:, h, :], xs[:, h, :] if h else h_ps[0][:, :], ACT.Copy)\
                   .then_inc(xs_hi_done, 1)

            first_hi(GATE)
            first_x_hi(0)
            first_xs_hi(0)
            first_hi(UP)
            first_hi(DOWN)

            def xs_hi_half(h, buf, halves_before):
                act.wait_ge(xs_done, halves_before + h + 1)
                act.activation(xs_hi[buf][:, h, :], xs[:, h, :], ACT.Copy).then_inc(xs_hi_done, 1)

            def w_hi_slice(n, buf, loads):
                act.wait_ge(w_loaded[buf], 3 * DMA * loads)
                act.activation(w_hi[buf][:, n, :, :], w_raw[buf][:, n, :, :], ACT.Copy)\
                   .then_inc(w_hi_done, 1)

            def expert(base, nxt, first=False):
                for k in range(UNITS):
                    act.wait_ge(gate_done, base + k + 1)
                    if not first or k >= 2:
                        act.wait_ge(hidden_done, base + k - 1)
                    act.activation(silu[k % 2][:, :], g_ps[k % BANKS][:, :], ACT.Silu)\
                       .then_inc(silu_done, 1)
                    if first and k == 1:
                        first_x_hi(1)
                    if first and k == 2:
                        first_xs_hi(1)
                    if nxt is None and k == UNITS - 1:
                        sum_to_sbuf(0)
                    if nxt is not None and k >= LAG:
                        buf, halves_before, loads = nxt
                        if k == LAG and not first:
                            act.wait_ge(down_done, base)
                        kind, n = PREPARE[k - LAG]
                        if kind == "slice":
                            w_hi_slice(n, buf, loads)
                        else:
                            xs_hi_half(n, buf, halves_before)
                    act.wait_ge(hidden_done, base + k + 1)
                    if not first or k >= HB:
                        act.wait_ge(down_done, base + k - HB + 1)
                    act.activation(h_hi[k % HB][:, :], h_ps[k % BANKS][:, :], ACT.Copy)\
                       .then_inc(h_hi_done, 1)

            expert(0, (1, 0, 1), first=True)
            with act.Fori(0, PAIRS - 1) as i:
                base = 2 * UNITS * i + UNITS
                expert(base, (0, 2 * HALVES * i + HALVES, i + 1))
                expert(base + UNITS, (1, 2 * HALVES * i + 2 * HALVES, i + 2))
            expert((E - 1) * UNITS, (0, (E - 1) * HALVES, PAIRS))
            def sum_to_sbuf(p):
                h, a, n = PIECES[p]
                act.wait_ge(down_done, LAST + 1 - NF * (HALVES - 1 - h))
                act.activation(y_t[:, h, a * S:(a + n) * S], y_ps[h][:, a * S:(a + n) * S], ACT.Copy)\
                   .then_inc(y_copied, 1)

            expert(E * UNITS, None)
            for p in range(1, len(PIECES)):
                sum_to_sbuf(p)

        @block.vector
        def _(dve):
            dve.memset(zeros[:, :], 0.0).then_inc(zeros_set, 1)

            def batches(t):
                return t.rearrange("p (b s) -> p b s", b=HBATCH)

            def shared_coef(h):
                c = coef[:, 0, h * HBATCH:(h + 1) * HBATCH]
                return c.unsqueeze(2).to_broadcast([P, HBATCH, P])

            def first_x_lo(h):
                dve.wait_ge(x_hi_done, h + 1)
                dve.tensor_tensor(x_lo[:, h, :], y_ps[h][:, :], f32(x_hi[:, h, :]), ALU.subtract)\
                   .then_inc(x_lo_done, 1)

            dve.wait_ge(sg_loaded, DMA)
            dve.tensor_copy(coef[:, 0, :], sg_sb[:, :]).then_inc(coef_ready, 1)
            dve.tensor_scalar(not_sg[:, :], sg_sb[:, :], -1.0, 1.0, ALU.mult, ALU.add)\
               .then_inc(one_minus, 1)
            dve.wait_ge(coef_ready, 1)
            dve.wait_ge(x_loaded[0], DMA)
            dve.tensor_tensor(xs_nat[:, :, :], half(x_nat, 0), shared_coef(0), ALU.mult)\
               .then_inc(xs_nat_done, 1)
            dve.wait_ge(first_w_hi_done, GATE + 1)
            dve.tensor_tensor(w_lo[0][:, :, GATE, :], w_raw[0][:, :, GATE, :],
                              f32(w_hi[0][:, :, GATE, :]), ALU.subtract).then_inc(first_gate_lo_done, 1)
            first_x_lo(0)
            dve.wait_ge(xs_hi_done, 1)
            dve.tensor_tensor(xs_lo[0][:, 0, :], h_ps[0][:, :], f32(xs_hi[0][:, 0, :]), ALU.subtract)\
               .then_inc(first_xs_lo_done, 1)
            dve.wait_ge(gates_loaded, DMA)
            dve.wait_ge(one_minus, 1)
            dve.tensor_tensor(coef[:, 1:, :].rearrange("p e b -> p b e"), gates_sb[:, :, :],
                              not_sg[:, :].unsqueeze(2).to_broadcast([P, B, E]), ALU.mult)\
               .then_inc(coef_ready, 1)

            def hidden(n, k, first=False):
                dve.wait_ge(silu_done, n + 1)
                dve.wait_ge(up_done, n + 1)
                if not first:
                    dve.wait_ge(h_lo_done, n - BANKS + 1)
                dve.tensor_tensor(h_ps[k % BANKS][:, :], silu[k % 2][:, :], u_ps[k % BANKS][:, :],
                                  ALU.mult).then_inc(hidden_done, 1)

            def hidden_lo(n, k):
                dve.wait_ge(h_hi_done, n + 1)
                dve.tensor_tensor(h_lo[k % HB][:, :], h_ps[k % BANKS][:, :], f32(h_hi[k % HB][:, :]),
                                  ALU.subtract).then_inc(h_lo_done, 1)

            for k in range(UNITS):
                hidden(k, k, first=k < BANKS)
                if k >= 1:
                    hidden_lo(k - 1, k - 1)
                if k == 1:
                    first_x_lo(1)
                    dve.tensor_tensor(batches(xs[:, 1, :]), batches(y_ps[1][:, :]), shared_coef(1),
                                      ALU.mult).then_inc(first_xs_done, 1)
                if k == 2:
                    dve.wait_ge(xs_hi_done, 2)
                    dve.wait_ge(first_xs_done, 1)
                    dve.tensor_tensor(xs_lo[0][:, 1, :], xs[:, 1, :], f32(xs_hi[0][:, 1, :]),
                                      ALU.subtract).then_inc(first_xs_lo_done, 1)
            with dve.Fori(1, E + 1) as e:
                for k in range(UNITS):
                    hidden(UNITS * e + k, k)
                    hidden_lo(UNITS * e + k - 1, (k - 1) % UNITS)
            hidden_lo(LAST, UNITS - 1)

            for p, (h, a, n) in enumerate(PIECES):
                b = h * HBATCH + a
                dve.wait_ge(y_transposed, p + 1)
                dve.tensor_tensor(out_sb[:, b:b + n, :],
                                  back_ps[p][:, 0:n * D].rearrange("p (b d) -> p b d", b=n),
                                  x_nat[:, b:b + n, :], ALU.add).then_inc(out_ready, 1)

        @block.tensor
        def _(pe):
            def warm_up(n):
                for _ in range(n):
                    pe.matmul(g_ps[1][:, :], zeros[:, 0:P], zeros[:, :], start=True, stop=True)

            pe.wait_ge(zeros_set, 1)
            warm_up(WARM_UP)
            pe.wait_ge(ident_built, 1)

            def transpose(tokens, bank, first, done):
                for b in range(HBATCH):
                    last = pe.transpose(bank[:, b * S:(b + 1) * S], tokens[:, first + b, :],
                                        ident[:, :])
                last.then_inc(done, 1)

            def down(n, k, buf, begin=False):
                f, h = k % NF, k // NF
                hi, lo = w_hi[buf][:, f, DOWN, :], w_lo[buf][:, f, DOWN, :]
                pe.wait_ge(h_hi_done, n + 1)
                pe.matmul(y_ps[h][:, :], hi, h_hi[k % HB][:, :], start=begin, stop=False,
                          skip_group_check=True)
                pe.matmul(y_ps[h][:, :], lo, h_hi[k % HB][:, :], start=False, stop=False,
                          skip_group_check=True)
                pe.wait_ge(h_lo_done, n + 1)
                pe.matmul(y_ps[h][:, :], hi, h_lo[k % HB][:, :], start=False,
                          stop=f == NF - 1, skip_group_check=True)\
                  .then_inc(down_done, 1)

            def shared_gate_unit(k):
                f, h = k % NF, k // NF
                g = g_ps[k % BANKS]
                if k >= BANKS:
                    pe.wait_ge(silu_done, k - BANKS + 1)
                pe.wait_ge(first_w_hi_done, GATE + 1)
                pe.wait_ge(x_hi_done, h + 1)
                pe.matmul(g[:, :], w_hi[0][:, f, GATE, :], x_hi[:, h, :], start=True, stop=False)
                pe.wait_ge(first_gate_lo_done, 1)
                pe.matmul(g[:, :], w_lo[0][:, f, GATE, :], x_hi[:, h, :], start=False, stop=False)
                pe.wait_ge(x_lo_done, h + 1)
                pe.matmul(g[:, :], w_hi[0][:, f, GATE, :], x_lo[:, h, :], start=False, stop=True)\
                  .then_inc(gate_done, 1)

            def shared_up_unit(k):
                f, h = k % NF, k // NF
                u = u_ps[k % BANKS]
                if k >= BANKS:
                    pe.wait_ge(hidden_done, k - BANKS + 1)
                pe.wait_ge(first_w_hi_done, UP + 1)
                pe.wait_ge(xs_hi_done, h + 1)
                pe.matmul(u[:, :], w_hi[0][:, f, UP, :], xs_hi[0][:, h, :], start=True, stop=False)
                pe.wait_ge(first_xs_lo_done, h + 1)
                pe.matmul(u[:, :], w_hi[0][:, f, UP, :], xs_lo[0][:, h, :], start=False, stop=False)
                pe.wait_ge(first_w_lo_done, min(f, 1) + 1)
                pe.matmul(u[:, :], w_lo[0][:, f, UP, :], xs_hi[0][:, h, :], start=False, stop=True)\
                  .then_inc(up_done, 1)

            pe.wait_ge(x_loaded[0], DMA)
            transpose(x_nat, y_ps[0], 0, x_transposed)
            pe.wait_ge(xs_nat_done, 1)
            transpose(xs_nat, h_ps[0], 0, xs_transposed)
            warm_up(WARM_UP_MORE)
            for k in range(BANKS):
                shared_gate_unit(k)
            for k in range(BANKS):
                shared_up_unit(k)
            pe.wait_ge(x_loaded[1], DMA)
            transpose(x_nat, y_ps[1], HBATCH, x_transposed)
            for k in range(BANKS, UNITS):
                shared_gate_unit(k)
                shared_up_unit(k)
                if k == BANKS:
                    pe.wait_ge(first_w_hi_done, DOWN + 1)
                    pe.wait_ge(first_w_lo_done, len(FIRST_LO))
                down(k - LAG, k - LAG, 0, begin=(k - LAG) % NF == 0)

            def routed_expert(base, buf, halves_before, slices_before):
                for k in range(UNITS):
                    f, h = k % NF, k // NF
                    g, u = g_ps[k % BANKS], u_ps[k % BANKS]
                    if h == 0:
                        pe.wait_ge(w_lo_done, slices_before + f + 1)
                    if f == 0:
                        pe.wait_ge(xs_lo_done, halves_before + h + 1)
                    pe.wait_ge(silu_done, base + k - BANKS + 1)
                    hi, lo = w_hi[buf][:, f, GATE, :], w_lo[buf][:, f, GATE, :]
                    pe.matmul(g[:, :], hi, x_hi[:, h, :], start=True, stop=False)
                    pe.matmul(g[:, :], hi, x_lo[:, h, :], start=False, stop=False)
                    pe.matmul(g[:, :], lo, x_hi[:, h, :], start=False, stop=True).then_inc(gate_done, 1)
                    pe.wait_ge(hidden_done, base + k - BANKS + 1)
                    hi, lo = w_hi[buf][:, f, UP, :], w_lo[buf][:, f, UP, :]
                    pe.matmul(u[:, :], hi, xs_hi[buf][:, h, :], start=True, stop=False)
                    pe.matmul(u[:, :], hi, xs_lo[buf][:, h, :], start=False, stop=False)
                    pe.matmul(u[:, :], lo, xs_hi[buf][:, h, :], start=False, stop=True)\
                      .then_inc(up_done, 1)
                    down(base + k - LAG, (k - LAG) % UNITS, buf if k >= LAG else 1 - buf)

            with pe.Fori(0, PAIRS) as i:
                for q in range(2):
                    routed_expert(2 * UNITS * i + UNITS * (q + 1), 1 - q,
                                  2 * HALVES * i + HALVES * q, 2 * NF * i + NF * q)
            def transpose_back(p):
                h, a, n = PIECES[p]
                pe.wait_ge(y_copied, p + 1)
                for b in range(n):
                    last = pe.transpose(back_ps[p][:, b * D:(b + 1) * D],
                                        y_t[:, h, (a + b) * S:(a + b + 1) * S], ident[:, :])
                last.then_inc(y_transposed, 1)

            pe.wait_ge(silu_done, LAST)
            transpose_back(0)
            down(LAST - 1, UNITS - 2, 0)
            down(LAST, UNITS - 1, 0)
            pe.wait_ge(silu_done, LAST + 1)
            pe.wait_ge(hidden_done, LAST)
            for p in range(1, len(PIECES)):
                transpose_back(p)


_INS = ["x", "fside_Bx8_0", "condB_sharedgateprob", "L0_cond_Wg", "L0_cond_Wu", "L0_cond_Wd",
        "L0_cond_Sg", "L0_cond_Su", "L0_cond_Sd"]


def kernel(**inputs):
    import numpy as _np
    import concourse.bacc as _bacc
    from concourse import mybir as _mybir
    from concourse.bass_utils import run_bass_kernel_spmd as _run

    nc = _bacc.Bacc("TRN2", target_bir_lowering=False, num_devices=1)
    arrays, args = {}, []
    for name in _INS:
        a = _np.ascontiguousarray(inputs[name])
        arrays[f"in_{name}"] = a
        args.append(nc.dram_tensor(f"in_{name}", a.shape, _mybir.dt.from_np(a.dtype),
                                   kind="ExternalInput").ap())
    shape = arrays["in_x"].shape
    out = nc.dram_tensor("out", shape, _mybir.dt.float32, kind="ExternalOutput").ap()
    build(nc, *args, out)
    r = _run(nc, [arrays], core_ids=[0])
    return r.results[0]["out"]
```

```python
from contextlib import ExitStack

import concourse.bass as bass
from concourse import mybir

FP32 = mybir.dt.float32
FP32R = mybir.dt.float32r
BF16 = mybir.dt.bfloat16
ALU = mybir.AluOpType
ACT = mybir.ActivationFunctionType

P = 128
HALVES = 2
LAG = 2
BANKS = 2
HB = 4
GATE, UP, DOWN = range(3)
DMA = 16
WARM_UP = 7


def build(nc, x, gates, shared_gate, Wg, Wu, Wd, Sg, Su, Sd, out):
    B, S, D = x.shape
    E, _, F = Wg.shape
    assert S == P and D == P and F % P == 0
    NF = F // P
    UNITS = NF * HALVES
    HBATCH = B // HALVES
    N = HBATCH * S
    PAIRS = E // 2
    LAST = (E + 1) * UNITS - 1
    PIECES = [(0, HBATCH // 2), (HBATCH // 2, HBATCH // 2)]
    PREPARE = [("slice", 0), ("half", 0)] + [("slice", n) for n in range(1, NF)] + [("half", 1)]
    FIRST_LO = [(UP, 0, 1), (UP, 1, NF), (DOWN, 0, NF)]
    assert E % 2 == 0 and UNITS % HB == 0 and UNITS % BANKS == 0
    assert LAG == BANKS and HB > LAG and UNITS == LAG + len(PREPARE)

    ctx = ExitStack()
    with ctx:
        def sbuf(name, shape, dtype):
            return ctx.enter_context(nc.sbuf_tensor(name, shape, dtype))

        def sem(name):
            return ctx.enter_context(nc.semaphore(name))

        x_nat = sbuf("x_nat", [P, B, D], FP32)
        x_t = sbuf("x_t", [P, HALVES, N], FP32)
        x_hi = sbuf("x_hi", [P, HALVES, N], FP32R)
        x_lo = sbuf("x_lo", [P, HALVES, N], FP32R)
        xs_nat = sbuf("xs_nat", [P, HBATCH, D], FP32)
        xs = sbuf("xs", [P, HALVES, N], FP32)
        xs_hi = [sbuf(f"xs_hi{i}", [P, HALVES, N], FP32R) for i in range(2)]
        xs_lo = [sbuf(f"xs_lo{i}", [P, HALVES, N], FP32R) for i in range(2)]
        w_raw = [sbuf(f"w_raw{i}", [P, 3, NF, P], FP32) for i in range(2)]
        w_hi = [sbuf(f"w_hi{i}", [P, 3, NF, P], FP32R) for i in range(2)]
        w_lo = [sbuf(f"w_lo{i}", [P, 3, NF, P], FP32R) for i in range(2)]
        silu = [sbuf(f"silu{i}", [P, N], FP32) for i in range(BANKS)]
        h_hi = [sbuf(f"h_hi{i}", [P, N], FP32R) for i in range(HB)]
        h_lo = [sbuf(f"h_lo{i}", [P, N], FP32R) for i in range(HB)]
        h_last = sbuf("h_last", [P, N], FP32)
        gates_sb = sbuf("gates_sb", [P, B, E], FP32)
        sg_sb = sbuf("sg_sb", [P, B], FP32)
        not_sg = sbuf("not_sg", [P, B], FP32)
        coef = sbuf("coef", [P, E + 1, B], FP32)
        ident = sbuf("ident", [P, P], FP32)
        zeros = sbuf("zeros", [P, N], BF16)
        table = sbuf("table", [P, 1], FP32)
        y_t = sbuf("y_t", [P, HALVES, N], FP32)
        out_sb = sbuf("out_sb", [P, B, D], FP32)

        def banks(name, n):
            return [ctx.enter_context(nc.psum_tensor(f"{name}{i}", [P, N], FP32)) for i in range(n)]

        y_ps = banks("y_ps", HALVES)
        g_ps = banks("g_ps", BANKS)
        u_ps = banks("u_ps", BANKS)
        h_ps = banks("h_ps", BANKS)
        back_ps = [g_ps[1], u_ps[0]]

        x_loaded = [sem(f"x_loaded{h}") for h in range(HALVES)]
        sg_loaded = sem("sg_loaded")
        gates_loaded = sem("gates_loaded")
        first_w_loaded = [sem(f"first_w_loaded{k}") for k in range(3)]
        w_loaded = [sem(f"w_loaded{i}") for i in range(2)]
        zeros_set = sem("zeros_set")
        ident_zeroed = sem("ident_zeroed")
        ident_built = sem("ident_built")
        one_minus = sem("one_minus")
        coef_ready = sem("coef_ready")
        x_transposed = sem("x_transposed")
        xs_nat_done = sem("xs_nat_done")
        xs_transposed = sem("xs_transposed")
        x_hi_done = sem("x_hi_done")
        x_lo_done = sem("x_lo_done")
        x_t_done = sem("x_t_done")
        first_xs_done = sem("first_xs_done")
        first_xs_lo_done = sem("first_xs_lo_done")
        first_w_hi_done = sem("first_w_hi_done")
        first_gate_lo_done = sem("first_gate_lo_done")
        first_w_lo_done = sem("first_w_lo_done")
        xs_done = sem("xs_done")
        xs_hi_done = sem("xs_hi_done")
        xs_lo_done = sem("xs_lo_done")
        w_hi_done = sem("w_hi_done")
        w_lo_done = sem("w_lo_done")
        gate_done = sem("gate_done")
        up_done = sem("up_done")
        silu_done = sem("silu_done")
        hidden_done = sem("hidden_done")
        h_hi_done = sem("h_hi_done")
        h_lo_done = sem("h_lo_done")
        down_done = sem("down_done")
        out_t_done = sem("out_t_done")
        out_transposed = sem("out_transposed")
        first_half_ready = sem("first_half_ready")
        y_copied = sem("y_copied")
        y_transposed = sem("y_transposed")
        out_ready = sem("out_ready")
        out_stored = sem("out_stored")

        x_view = x.rearrange("b s d -> s b d")
        out_view = out.rearrange("b s d -> s b d")

        def half(t, h):
            return t[:, h * HBATCH:(h + 1) * HBATCH, :]

        def in_slices(w):
            return w.rearrange("d (n j) -> d n j", j=P)

        def in_rows(w):
            return w.rearrange("(n p) d -> p n d", p=P)

        def f32(t):
            return t.bitcast(FP32)

        block = ctx.enter_context(nc.Block())

        @block.sync
        def _(sp):
            sp.dma_start(half(x_nat, 0), half(x_view, 0)).then_inc(x_loaded[0], DMA)
            sp.dma_start(w_raw[0][:, UP, :, :], in_slices(Su)).then_inc(first_w_loaded[UP], DMA)
            sp.dma_start(w_raw[0][:, DOWN, :, :], in_rows(Sd)).then_inc(first_w_loaded[DOWN], DMA)
            sp.dma_start(half(x_nat, 1), half(x_view, 1)).then_inc(x_loaded[1], DMA)

            def load_expert(r, buf):
                sp.dma_start(w_raw[buf][:, GATE, :, :], in_slices(Wg[r])).then_inc(w_loaded[buf], DMA)
                sp.dma_start(w_raw[buf][:, UP, :, :], in_slices(Wu[r])).then_inc(w_loaded[buf], DMA)
                sp.dma_start(w_raw[buf][:, DOWN, :, :], in_rows(Wd[r])).then_inc(w_loaded[buf], DMA)

            load_expert(0, 1)
            sp.wait_ge(first_w_hi_done, 3)
            sp.wait_ge(first_gate_lo_done, 1)
            sp.wait_ge(first_w_lo_done, len(FIRST_LO))
            load_expert(1, 0)
            with sp.Fori(0, PAIRS - 1) as i:
                sp.wait_ge(w_lo_done, 2 * NF * i + NF)
                load_expert(2 * i + 2, 1)
                sp.wait_ge(w_lo_done, 2 * NF * i + 2 * NF)
                load_expert(2 * i + 3, 0)

            sp.wait_ge(first_half_ready, 1)
            sp.dma_start(half(out_view, 0), half(out_sb, 0)).then_inc(out_stored, DMA)
            sp.wait_ge(out_ready, len(PIECES))
            sp.dma_start(half(out_view, 1), half(out_sb, 1)).then_inc(out_stored, DMA)
            sp.wait_ge(out_stored, HALVES * DMA)

        @block.gpsimd
        def _(pool):
            pool.dma_start(sg_sb[:, :], shared_gate.partition_broadcast(P)).then_inc(sg_loaded, DMA)
            pool.memset(ident[:, :], 0.0).then_inc(ident_zeroed, 1)
            pool.wait_ge(ident_zeroed, 1)
            pool.affine_select(out=ident[:, :], in_=ident[:, :], compare_op=ALU.not_equal, fill=1.0,
                               base=0, pattern=[[-1, P]], channel_multiplier=1).then_inc(ident_built, 1)
            pool.dma_start(gates_sb[:, :, :], gates.partition_broadcast(P)).then_inc(gates_loaded, DMA)
            for k, n, m in FIRST_LO:
                pool.wait_ge(first_w_hi_done, k + 1)
                pool.tensor_tensor(w_lo[0][:, k, n:m, :], w_raw[0][:, k, n:m, :],
                                   f32(w_hi[0][:, k, n:m, :]), ALU.subtract).then_inc(first_w_lo_done, 1)
            def tokens(h):
                pool.wait_ge(x_hi_done, h + 1)
                pool.wait_ge(x_lo_done, h + 1)
                pool.tensor_tensor(x_t[:, h, :], f32(x_hi[:, h, :]), f32(x_lo[:, h, :]), ALU.add)\
                    .then_inc(x_t_done, 1)

            def prepare(e, buf, halves_before, slices_before, second):
                for h in range(HALVES):
                    if not second:
                        tokens(h)
                        pool.wait_ge(x_t_done, h + 1)
                    pool.wait_ge(xs_hi_done, halves_before + h + 1)
                    if second:
                        pool.wait_ge(xs_lo_done, halves_before - HALVES + h + 1)
                    else:
                        pool.wait_ge(first_xs_lo_done, h + 1)
                    c = coef[:, e, h * HBATCH:(h + 1) * HBATCH]
                    pool.tensor_tensor(
                        xs[:, h, :].rearrange("p (b s) -> p b s", b=HBATCH),
                        x_t[:, h, :].rearrange("p (b s) -> p b s", b=HBATCH),
                        c.unsqueeze(2).to_broadcast([P, HBATCH, S]), ALU.mult).then_inc(xs_done, 1)

                def slice_lo(n):
                    pool.wait_ge(w_hi_done, slices_before + n + 1)
                    pool.tensor_tensor(w_lo[buf][:, :, n, :], w_raw[buf][:, :, n, :],
                                       f32(w_hi[buf][:, :, n, :]), ALU.subtract).then_inc(w_lo_done, 1)

                def half_lo(h):
                    pool.wait_ge(xs_hi_done, halves_before + HALVES + h + 1)
                    pool.tensor_tensor(xs_lo[buf][:, h, :], xs[:, h, :], f32(xs_hi[buf][:, h, :]),
                                       ALU.subtract).then_inc(xs_lo_done, 1)

                for kind, n in PREPARE:
                    (slice_lo if kind == "slice" else half_lo)(n)

            pool.wait_ge(coef_ready, 2)
            prepare(1, 1, 0, 0, second=False)
            with pool.Fori(0, PAIRS - 1) as i:
                for q in range(2):
                    prepare(2 * i + 2 + q, q, 2 * HALVES * i + HALVES * (q + 1),
                            2 * NF * i + NF * (q + 1), second=True)
            prepare(E, 0, HALVES * (E - 1), NF * (E - 1), second=True)

        @block.scalar
        def _(act):
            act.dma_start(w_raw[0][:, GATE, :, :], in_slices(Sg)).then_inc(first_w_loaded[GATE], DMA)
            act.wait_ge(zeros_set, 1)
            act.activation(table[:, :], zeros[:, 0:1], ACT.Silu)

            def first_hi(k):
                act.wait_ge(first_w_loaded[k], DMA)
                act.activation(w_hi[0][:, k, :, :], w_raw[0][:, k, :, :], ACT.Copy)\
                   .then_inc(first_w_hi_done, 1)

            def first_x_hi(h):
                act.wait_ge(x_transposed, h + 1)
                act.activation(x_hi[:, h, :], y_ps[h][:, :], ACT.Copy).then_inc(x_hi_done, 1)

            def first_xs_hi(h):
                act.wait_ge(first_xs_done if h else xs_transposed, 1)
                act.activation(xs_hi[0][:, h, :], xs[:, h, :] if h else h_ps[0][:, :], ACT.Copy)\
                   .then_inc(xs_hi_done, 1)

            first_hi(GATE)
            first_x_hi(0)
            first_xs_hi(0)
            first_hi(UP)
            first_hi(DOWN)

            def xs_hi_half(h, buf, halves_before):
                act.wait_ge(xs_done, halves_before + h + 1)
                act.activation(xs_hi[buf][:, h, :], xs[:, h, :], ACT.Copy).then_inc(xs_hi_done, 1)

            def w_hi_slice(n, buf, loads):
                act.wait_ge(w_loaded[buf], 3 * DMA * loads)
                act.activation(w_hi[buf][:, :, n, :], w_raw[buf][:, :, n, :], ACT.Copy)\
                   .then_inc(w_hi_done, 1)

            def silu_of(n, k):
                act.wait_ge(gate_done, n + 1)
                act.activation(silu[k % BANKS][:, :], g_ps[k % BANKS][:, :], ACT.Silu)\
                   .then_inc(silu_done, 1)

            def hidden_hi(n, k):
                act.wait_ge(hidden_done, n + 1)
                act.activation(h_hi[k % HB][:, :], h_ps[k % BANKS][:, :], ACT.Copy)\
                   .then_inc(h_hi_done, 1)

            def split_next(k, buf, halves_before, loads):
                kind, n = PREPARE[k - LAG]
                if kind == "slice":
                    w_hi_slice(n, buf, loads)
                else:
                    xs_hi_half(n, buf, halves_before)

            def routed_units(base, nxt):
                for k in range(UNITS):
                    silu_of(base + k, k)
                    if nxt is not None and k == LAG:
                        act.wait_ge(down_done, base)
                    if nxt is not None and k >= LAG:
                        split_next(k, *nxt)
                    if nxt is not None or k < UNITS - 1:
                        hidden_hi(base + k, k)

            for k in range(BANKS):
                silu_of(k, k)
            hidden_hi(0, 0)
            first_x_hi(1)
            hidden_hi(1, 1)
            for k in range(BANKS, UNITS):
                silu_of(k, k)
                if k == BANKS:
                    first_xs_hi(1)
                split_next(k, 1, 0, 1)
                hidden_hi(k, k)

            with act.Fori(0, PAIRS - 1) as i:
                base = 2 * UNITS * i + UNITS
                routed_units(base, (0, 2 * HALVES * i + HALVES, i + 1))
                routed_units(base + UNITS, (1, 2 * HALVES * i + 2 * HALVES, i + 2))
            routed_units((E - 1) * UNITS, (0, (E - 1) * HALVES, PAIRS))
            routed_units(E * UNITS, None)
            act.wait_ge(down_done, LAST + 1)
            for a, n in PIECES:
                act.activation(y_t[:, 1, a * S:(a + n) * S], y_ps[1][:, a * S:(a + n) * S], ACT.Copy)\
                   .then_inc(y_copied, 1)
            act.wait_ge(out_transposed, 1)
            act.activation(half(out_sb, 0), g_ps[0][:, :].rearrange("p (b d) -> p b d", b=HBATCH),
                           ACT.Copy).then_inc(first_half_ready, 1)

        @block.vector
        def _(dve):
            dve.memset(zeros[:, :], 0.0).then_inc(zeros_set, 1)

            def batches(t):
                return t.rearrange("p (b s) -> p b s", b=HBATCH)

            def shared_coef(h):
                c = coef[:, 0, h * HBATCH:(h + 1) * HBATCH]
                return c.unsqueeze(2).to_broadcast([P, HBATCH, P])

            def first_x_lo(h):
                dve.wait_ge(x_hi_done, h + 1)
                dve.tensor_tensor(x_lo[:, h, :], y_ps[h][:, :], f32(x_hi[:, h, :]), ALU.subtract)\
                   .then_inc(x_lo_done, 1)

            dve.wait_ge(sg_loaded, DMA)
            dve.tensor_copy(coef[:, 0, :], sg_sb[:, :]).then_inc(coef_ready, 1)
            dve.tensor_scalar(not_sg[:, :], sg_sb[:, :], -1.0, 1.0, ALU.mult, ALU.add)\
               .then_inc(one_minus, 1)
            dve.wait_ge(coef_ready, 1)
            dve.wait_ge(x_loaded[0], DMA)
            dve.tensor_tensor(xs_nat[:, :, :], half(x_nat, 0), shared_coef(0), ALU.mult)\
               .then_inc(xs_nat_done, 1)
            dve.wait_ge(first_w_hi_done, GATE + 1)
            dve.tensor_tensor(w_lo[0][:, GATE, :, :], w_raw[0][:, GATE, :, :],
                              f32(w_hi[0][:, GATE, :, :]), ALU.subtract).then_inc(first_gate_lo_done, 1)
            first_x_lo(0)
            dve.wait_ge(xs_hi_done, 1)
            dve.tensor_tensor(xs_lo[0][:, 0, :], h_ps[0][:, :], f32(xs_hi[0][:, 0, :]), ALU.subtract)\
               .then_inc(first_xs_lo_done, 1)
            dve.wait_ge(gates_loaded, DMA)
            dve.wait_ge(one_minus, 1)
            dve.tensor_tensor(coef[:, 1:, :].rearrange("p e b -> p b e"), gates_sb[:, :, :],
                              not_sg[:, :].unsqueeze(2).to_broadcast([P, B, E]), ALU.mult)\
               .then_inc(coef_ready, 1)

            def hidden(n, k, first=False, to=None):
                dve.wait_ge(silu_done, n + 1)
                dve.wait_ge(up_done, n + 1)
                if not first:
                    dve.wait_ge(h_lo_done, n - BANKS + 1)
                dve.tensor_tensor((to or h_ps[k % BANKS])[:, :], silu[k % BANKS][:, :], u_ps[k % BANKS][:, :],
                                  ALU.mult).then_inc(hidden_done, 1)

            def hidden_lo(n, k):
                dve.wait_ge(h_hi_done, n + 1)
                dve.tensor_tensor(h_lo[k % HB][:, :], h_ps[k % BANKS][:, :], f32(h_hi[k % HB][:, :]),
                                  ALU.subtract).then_inc(h_lo_done, 1)

            hidden(0, 0, first=True)
            hidden(1, 1, first=True)
            hidden_lo(0, 0)
            first_x_lo(1)
            dve.tensor_tensor(batches(xs[:, 1, :]), batches(y_ps[1][:, :]), shared_coef(1),
                              ALU.mult).then_inc(first_xs_done, 1)
            for k in range(2, UNITS):
                hidden(k, k)
                hidden_lo(k - 1, k - 1)
                if k == 2:
                    dve.wait_ge(xs_hi_done, 2)
                    dve.wait_ge(first_xs_done, 1)
                    dve.tensor_tensor(xs_lo[0][:, 1, :], xs[:, 1, :], f32(xs_hi[0][:, 1, :]),
                                      ALU.subtract).then_inc(first_xs_lo_done, 1)
            with dve.Fori(1, E) as e:
                for k in range(UNITS):
                    hidden(UNITS * e + k, k)
                    hidden_lo(UNITS * e + k - 1, (k - 1) % UNITS)
            for k in range(UNITS - 1):
                if k == UNITS - 2:
                    dve.wait_ge(down_done, LAST + 1 - NF)
                    dve.wait_ge(x_t_done, 1)
                    dve.tensor_tensor(y_t[:, 0, :], y_ps[0][:, :], x_t[:, 0, :], ALU.add)\
                       .then_inc(out_t_done, 1)
                hidden(UNITS * E + k, k)
                hidden_lo(UNITS * E + k - 1, (k - 1) % UNITS)
            hidden_lo(LAST - 1, UNITS - 2)
            hidden(LAST, UNITS - 1, to=h_last)

            for p, (a, n) in enumerate(PIECES):
                b = HBATCH + a
                dve.wait_ge(y_transposed, p + 1)
                dve.tensor_tensor(out_sb[:, b:b + n, :],
                                  back_ps[p][:, 0:n * D].rearrange("p (b d) -> p b d", b=n),
                                  x_nat[:, b:b + n, :], ALU.add).then_inc(out_ready, 1)

        @block.tensor
        def _(pe):
            pe.wait_ge(zeros_set, 1)
            for _ in range(WARM_UP):
                pe.matmul(g_ps[1][:, :], zeros[:, 0:P], zeros[:, :], start=True, stop=True)
            pe.wait_ge(ident_built, 1)

            def transpose(tokens, bank, first, done):
                for b in range(HBATCH):
                    last = pe.transpose(bank[:, b * S:(b + 1) * S], tokens[:, first + b, :],
                                        ident[:, :])
                last.then_inc(done, 1)

            def down(n, k, buf, begin=False):
                f, h = k % NF, k // NF
                hi, lo = w_hi[buf][:, DOWN, f, :], w_lo[buf][:, DOWN, f, :]
                pe.wait_ge(h_hi_done, n + 1)
                pe.matmul(y_ps[h][:, :], lo, h_hi[k % HB][:, :], start=begin, stop=False,
                          skip_group_check=True)
                pe.matmul(y_ps[h][:, :], hi, h_hi[k % HB][:, :], start=False, stop=False,
                          skip_group_check=True)
                pe.wait_ge(h_lo_done, n + 1)
                pe.matmul(y_ps[h][:, :], hi, h_lo[k % HB][:, :], start=False,
                          stop=f == NF - 1, skip_group_check=True)\
                  .then_inc(down_done, 1)

            def shared_gate_unit(k):
                f, h = k % NF, k // NF
                g = g_ps[k % BANKS]
                if k >= BANKS:
                    pe.wait_ge(silu_done, k - BANKS + 1)
                pe.wait_ge(first_w_hi_done, GATE + 1)
                pe.wait_ge(x_hi_done, h + 1)
                pe.matmul(g[:, :], w_hi[0][:, GATE, f, :], x_hi[:, h, :], start=True, stop=False)
                pe.wait_ge(first_gate_lo_done, 1)
                pe.matmul(g[:, :], w_lo[0][:, GATE, f, :], x_hi[:, h, :], start=False, stop=False)
                pe.wait_ge(x_lo_done, h + 1)
                pe.matmul(g[:, :], w_hi[0][:, GATE, f, :], x_lo[:, h, :], start=False, stop=True)\
                  .then_inc(gate_done, 1)

            def shared_up_unit(k):
                f, h = k % NF, k // NF
                u = u_ps[k % BANKS]
                if k >= BANKS:
                    pe.wait_ge(hidden_done, k - BANKS + 1)
                pe.wait_ge(first_w_hi_done, UP + 1)
                pe.wait_ge(xs_hi_done, h + 1)
                pe.matmul(u[:, :], w_hi[0][:, UP, f, :], xs_hi[0][:, h, :], start=True, stop=False)
                pe.wait_ge(first_xs_lo_done, h + 1)
                pe.matmul(u[:, :], w_hi[0][:, UP, f, :], xs_lo[0][:, h, :], start=False, stop=False)
                pe.wait_ge(first_w_lo_done, min(f, 1) + 1)
                pe.matmul(u[:, :], w_lo[0][:, UP, f, :], xs_hi[0][:, h, :], start=False, stop=True)\
                  .then_inc(up_done, 1)

            pe.wait_ge(x_loaded[0], DMA)
            transpose(x_nat, y_ps[0], 0, x_transposed)
            pe.wait_ge(xs_nat_done, 1)
            transpose(xs_nat, h_ps[0], 0, xs_transposed)
            for k in range(BANKS):
                shared_gate_unit(k)
            for k in range(BANKS):
                shared_up_unit(k)
            pe.wait_ge(x_loaded[1], DMA)
            transpose(x_nat, y_ps[1], HBATCH, x_transposed)
            for k in range(BANKS, UNITS):
                shared_gate_unit(k)
                shared_up_unit(k)
                if k == BANKS:
                    pe.wait_ge(first_w_hi_done, DOWN + 1)
                    pe.wait_ge(first_w_lo_done, len(FIRST_LO))
                down(k - LAG, k - LAG, 0, begin=(k - LAG) % NF == 0)

            def routed_expert(base, buf, halves_before, slices_before):
                for k in range(UNITS):
                    f, h = k % NF, k // NF
                    g, u = g_ps[k % BANKS], u_ps[k % BANKS]
                    if h == 0:
                        pe.wait_ge(w_lo_done, slices_before + f + 1)
                    if f == 0:
                        pe.wait_ge(xs_lo_done, halves_before + h + 1)
                    pe.wait_ge(silu_done, base + k - BANKS + 1)
                    hi, lo = w_hi[buf][:, GATE, f, :], w_lo[buf][:, GATE, f, :]
                    pe.matmul(g[:, :], hi, x_hi[:, h, :], start=True, stop=False)
                    pe.matmul(g[:, :], hi, x_lo[:, h, :], start=False, stop=False)
                    pe.matmul(g[:, :], lo, x_hi[:, h, :], start=False, stop=True).then_inc(gate_done, 1)
                    pe.wait_ge(hidden_done, base + k - BANKS + 1)
                    hi, lo = w_hi[buf][:, UP, f, :], w_lo[buf][:, UP, f, :]
                    pe.matmul(u[:, :], hi, xs_hi[buf][:, h, :], start=True, stop=False)
                    pe.matmul(u[:, :], hi, xs_lo[buf][:, h, :], start=False, stop=False)
                    pe.matmul(u[:, :], lo, xs_hi[buf][:, h, :], start=False, stop=True)\
                      .then_inc(up_done, 1)
                    down(base + k - LAG, (k - LAG) % UNITS, buf if k >= LAG else 1 - buf)

            with pe.Fori(0, PAIRS) as i:
                for q in range(2):
                    routed_expert(2 * UNITS * i + UNITS * (q + 1), 1 - q,
                                  2 * HALVES * i + HALVES * q, 2 * NF * i + NF * q)
            def transpose_back(h, a, n, bank, done):
                for b in range(n):
                    last = pe.transpose(bank[:, b * D:(b + 1) * D],
                                        y_t[:, h, (a + b) * S:(a + b + 1) * S], ident[:, :])
                last.then_inc(done, 1)

            down(LAST - 1, UNITS - 2, 0)
            pe.wait_ge(hidden_done, LAST + 1)
            pe.matmul(y_ps[1][:, :], w_raw[0][:, DOWN, NF - 1, :], h_last[:, :], start=False, stop=True,
                      skip_group_check=True).then_inc(down_done, 1)
            pe.wait_ge(out_t_done, 1)
            transpose_back(0, 0, HBATCH, g_ps[0], out_transposed)
            for p, (a, n) in enumerate(PIECES):
                pe.wait_ge(y_copied, p + 1)
                transpose_back(1, a, n, back_ps[p], y_transposed)


_INS = ["x", "fside_Bx8_0", "condB_sharedgateprob", "L0_cond_Wg", "L0_cond_Wu", "L0_cond_Wd",
        "L0_cond_Sg", "L0_cond_Su", "L0_cond_Sd"]


def kernel(**inputs):
    import numpy as _np
    import concourse.bacc as _bacc
    from concourse import mybir as _mybir
    from concourse.bass_utils import run_bass_kernel_spmd as _run

    nc = _bacc.Bacc("TRN2", target_bir_lowering=False, num_devices=1)
    arrays, args = {}, []
    for name in _INS:
        a = _np.ascontiguousarray(inputs[name])
        arrays[f"in_{name}"] = a
        args.append(nc.dram_tensor(f"in_{name}", a.shape, _mybir.dt.from_np(a.dtype),
                                   kind="ExternalInput").ap())
    shape = arrays["in_x"].shape
    out = nc.dram_tensor("out", shape, _mybir.dt.float32, kind="ExternalOutput").ap()
    build(nc, *args, out)
    r = _run(nc, [arrays], core_ids=[0])
    return r.results[0]["out"]
```
